# Optimizing a Trainium2 kernel written in Bass

```python
import numpy as np
import jax
import jax.numpy as jnp

def _softmax(x, axis=-1):
    return jax.nn.softmax(x, axis=axis)

def _gelu(x):
    return jax.nn.gelu(x, approximate=True)

def _silu(x):
    return jax.nn.silu(x)

def _sigmoid(x):
    return jax.nn.sigmoid(x)

def _layernorm(x, axis=-1, eps=1e-05):
    m = jnp.mean(x, axis=axis, keepdims=True)
    v = jnp.var(x, axis=axis, keepdims=True)
    return (x - m) / jnp.sqrt(v + eps)

def _scatter_add(tgt, idx, src, axis=0):
    return tgt.at[idx].add(src)

def _segment_sum(src, seg, n):
    return jax.ops.segment_sum(src, seg, n)
kernel_name = 'mk_cond_resid_d2_seqx_r8_34a0f2'

def setup_inputs(seed: int=0):
    np.random.seed(seed)
    _w = jnp.asarray

    def _rec_inputs():
        import jax
        import jax.numpy as jnp
        _rk = jax.random.key(seed)
        x = -8.015e-05 + 0.9999 * jax.random.normal(jax.random.fold_in(_rk, 1), (32, 32, 256), jnp.float32)
        _lenS = 32 - jax.random.randint(jax.random.fold_in(_rk, 7), (32,), 0, max(1, 32 // 4) + 1, jnp.int32)
        _lenS2 = 32 - jax.random.randint(jax.random.fold_in(_rk, 8), (32,), 0, max(1, 32 // 4) + 1, jnp.int32)
        cond_1024 = 0.00191187 + 0.999416 * jax.random.normal(jax.random.fold_in(_rk, 11), (32, 128), jnp.float32)
        return (x, cond_1024)
    x, cond_1024 = _rec_inputs()

    def _L0_cond_setup():
        import jax, jax.numpy as jnp
        import numpy as np
        B, N, V_DIM, Q_DIM = (32, 100, 256, 128)
        key = jax.random.key(seed)
        k1, k2, k3, k4 = jax.random.split(key, 4)
        v = jax.random.normal(k1, (B, N, V_DIM), dtype=jnp.float32)
        q = jax.random.normal(k2, (B, Q_DIM), dtype=jnp.float32)
        W3 = jax.random.normal(k3, (Q_DIM, V_DIM), dtype=jnp.float32) * (1.0 / np.sqrt(Q_DIM))
        b3 = jnp.zeros((V_DIM,), dtype=jnp.float32)
        W2 = jax.random.normal(k4, (V_DIM, V_DIM), dtype=jnp.float32) * (1.0 / np.sqrt(V_DIM))
        b2 = jnp.zeros((V_DIM,), dtype=jnp.float32)
        return {'v': v, 'q': q, 'W3': W3, 'b3': b3, 'W2': W2, 'b2': b2}
    _L0_cond_all = _L0_cond_setup()
    _L0_cond_in = {k: v for k, v in _L0_cond_all.items() if k in ('W3', 'b3', 'W2', 'b2')}
    del _L0_cond_all

    def _L1_cond_setup():
        import jax, jax.numpy as jnp
        import numpy as np
        N, B, D, Q = (32, 36, 256, 128)
        key = jax.random.key(seed)
        ks = jax.random.split(key, 6)
        sc = 0.02
        return {'v': jax.random.normal(ks[0], (N, B, D), jnp.float32), 'q': jax.random.normal(ks[1], (N, Q), jnp.float32), 'W1': jax.random.normal(ks[2], (D, D), jnp.float32) * sc, 'b1': jnp.zeros((D,), jnp.float32), 'W2': jax.random.normal(ks[3], (D, D), jnp.float32) * sc, 'b2': jnp.zeros((D,), jnp.float32), 'W3': jax.random.normal(ks[4], (Q, D), jnp.float32) * sc, 'b3': jnp.zeros((D,), jnp.float32)}
    _L1_cond_all = _L1_cond_setup()
    _L1_cond_in = {k: v for k, v in _L1_cond_all.items() if k in ('W1', 'b1', 'W2', 'b2', 'W3', 'b3')}
    del _L1_cond_all
    return {'x': x, 'cond_1024': cond_1024, 'L0_cond_W3': _L0_cond_in['W3'], 'L0_cond_b3': _L0_cond_in['b3'], 'L0_cond_W2': _L0_cond_in['W2'], 'L0_cond_b2': _L0_cond_in['b2'], 'L1_cond_W1': _L1_cond_in['W1'], 'L1_cond_b1': _L1_cond_in['b1'], 'L1_cond_W2': _L1_cond_in['W2'], 'L1_cond_b2': _L1_cond_in['b2'], 'L1_cond_W3': _L1_cond_in['W3'], 'L1_cond_b3': _L1_cond_in['b3']}

def reference(x, cond_1024, L0_cond_W3, L0_cond_b3, L0_cond_W2, L0_cond_b2, L1_cond_W1, L1_cond_b1, L1_cond_W2, L1_cond_b2, L1_cond_W3, L1_cond_b3):
    import jax
    import jax.numpy as jnp

    def _L0_cond_ref(v, q, W3, b3, W2, b2):
        import jax, jax.numpy as jnp
        import numpy as np
        B, N, V_DIM, Q_DIM = (32, 100, 256, 128)
        q_emb = jax.nn.relu(q @ W3 + b3)
        n = v.shape[1]
        v_sum = jnp.sum(v, axis=1, keepdims=True)
        x = (n * v + v_sum) * q_emb[:, None, :]
        return jax.nn.relu(x @ W2 + b2)

    def _L1_cond_ref(v, q, W1, b1, W2, b2, W3, b3):
        import jax, jax.numpy as jnp
        import numpy as np
        N, B, D, Q = (32, 36, 256, 128)
        qe = jax.nn.relu(q @ W3 + b3)
        pairs = (v[:, :, None, :] + v[:, None, :, :]) * qe[:, None, None, :]
        h = jax.nn.relu(jnp.einsum('nijd,de->nije', pairs, W1) + b1)
        x = jnp.sum(h, axis=2)
        return jax.nn.relu(x @ W2 + b2)
    x = x + _L0_cond_ref(x, cond_1024, L0_cond_W3, L0_cond_b3, L0_cond_W2, L0_cond_b2)
    x = x + _L1_cond_ref(x, cond_1024, L1_cond_W1, L1_cond_b1, L1_cond_W2, L1_cond_b2, L1_cond_W3, L1_cond_b3)
    return x

_drawn_inputs = setup_inputs


def setup_inputs(seed=0):
    import zlib

    import numpy as np

    out = dict(_drawn_inputs(seed))
    spreads = {'L0_cond_b3': (0.0, 0.1),
     'L0_cond_b2': (0.0, 2.0),
     'L1_cond_b1': (0.0, 0.365),
     'L1_cond_b2': (0.0, 2.0),
     'L1_cond_b3': (0.0, 0.1)}
    factors = {}
    for name, (base, spread) in spreads.items():
        noise = np.random.default_rng([zlib.crc32(name.encode()), seed]).standard_normal(out[name].shape)
        drawn = base * np.exp(spread * noise) if base else spread * noise
        out[name] = jnp.asarray(drawn.astype(out[name].dtype))
    for name, factor in factors.items():
        out[name] = (out[name] * factor).astype(out[name].dtype)
    return out
```

```python
from contextlib import ExitStack

import concourse.bass as bass
from concourse import mybir

F32 = mybir.dt.float32
BF16 = mybir.dt.bfloat16
ALU = mybir.AluOpType
ACT = mybir.ActivationFunctionType

P = 128
BATCHES, N, D, Q = 32, 32, 256, 128
KD = D // P
STRIPS = P // N
TILES = BATCHES // STRIPS
PER = 2
GROUPS = TILES // PER
W = PER * D
GB = PER * STRIPS
CHUNKS = 4
PAIRS = N * (N - 1) // 2
PC = PAIRS // CHUNKS
PARTS = 3
K3 = PARTS * N
QUADS = GROUPS * CHUNKS
RING = 2
WARM = 10

LEAD = [("mix", 1), ("lin0", 0), ("mix", 2), ("turn1", 0), ("lin0", 1), ("lin1", 0), ("mix", 3),
        ("turn1", 1), ("lin0", 2), ("lin1", 1)]
BETWEEN = {0: [("turn1", 2), ("lin0", 3)], 2: [("lin1", 2)], 3: [("turn1", 3)], 4: [("lin1", 3)],
           5: [("turn2", 0)], 6: [("lin2", 0)], 9: [("turn2", 1)], 10: [("lin2", 1)], 13: [("turn2", 2)]}
LAST = GROUPS - 1


def on_scalar(k, s):
    return s != 3


def relus(k, s, scalar):
    return sum(on_scalar(kk, ss) == scalar for kk in range(k + 1) for ss in range(STRIPS)
               if kk < k or ss <= s)


def build(nc, x, q_pack, w3_1, biases, w_lin, squares, pick_m, gather_m, out):
    ctx = ExitStack()
    with ctx:
        def sb(name, shape, dt=F32):
            return ctx.enter_context(nc.sbuf_tensor(name, shape, dt))

        def bank(name):
            return ctx.enter_context(nc.psum_tensor(name, [P, W], F32))

        def sem(name):
            return ctx.enter_context(nc.semaphore(name))

        x_sb = sb("x_sb", [P, GROUPS, W])
        q_sb = sb("q_sb", [Q, BATCHES + 2 * KD + D])
        w31_sb = sb("w31_sb", [Q, D])
        wl_sb = sb("wl_sb", [P, 3, KD, D])
        b_sb = sb("b_sb", [P, 3, D])
        half_b1 = sb("half_b1", [P, D])
        sq_sb = sb("sq_sb", [P, 2, P])
        warm_sb = sb("warm_sb", [P, W], BF16)
        pick_sb = sb("pick_sb", [K3, CHUNKS, P], BF16)
        gather_sb = sb("gather_sb", [P, CHUNKS, N])
        qe = sb("qe", [P, 2, KD, BATCHES])
        q_lin = sb("q_lin", [P, 2, KD, BATCHES])
        zT = sb("zT", [P, GROUPS, W])
        y0 = sb("y0", [P, GROUPS, W])
        x1 = sb("x1", [P, GROUPS, W])
        uT = sb("uT", [P, GROUPS, W])
        a = sb("a", [P, GROUPS, W])
        a_parts = sb("a_parts", [P, GROUPS, PARTS, W], BF16)
        a_hi, a_mid, a_lo = (a_parts[:, :, part, :] for part in range(PARTS))
        a_rest = sb("a_rest", [P, GROUPS, W])
        diag = sb("diag", [P, GROUPS, W])
        a3 = sb("a3", [K3, GROUPS, STRIPS, W], BF16)
        h = sb("h", [P, RING * STRIPS, W])
        x2 = sb("x2", [P, GROUPS, W])
        x2T = sb("x2T", [P, GROUPS, W])
        y1 = sb("y1", [P, GROUPS, W])
        y = sb("y", [P, GROUPS, W])

        z_ps = [bank(f"z_ps{s}") for s in range(STRIPS)]
        sum_ps = bank("sum_ps")
        turn_ps = bank("turn_ps")
        lin_ps = bank("lin_ps")
        end_ps = bank("end_ps")

        s_x = [sem(f"s_x_in{g}") for g in range(GROUPS)]
        s_q = sem("s_q")
        s_w31 = sem("s_w31")
        s_sq = sem("s_sq")
        s_wl = [sem(f"s_wl{n}") for n in range(3)]
        s_b = sem("s_b")
        s_pick = sem("s_pick")
        s_a3 = [sem(f"s_a3_{g}") for g in range(GROUPS)]
        s_out = sem("s_out")
        s_warm = sem("s_warm")
        s_qe_ps = sem("s_qe_ps")
        s_mixed = sem("s_mixed")
        s_lin0 = sem("s_lin0")
        s_turn1 = sem("s_turn1")
        s_lin1 = sem("s_lin1")
        s_z = sem("s_z")
        s_sum = sem("s_sum")
        s_turn2 = sem("s_turn2")
        s_lin2 = sem("s_lin2")
        s_q_lin = sem("s_q_lin")
        s_qe = sem("s_qe")
        s_zT = sem("s_zT")
        s_half = sem("s_half")
        s_y0 = sem("s_y0")
        s_x1 = sem("s_x1")
        s_uT = sem("s_uT")
        s_a = sem("s_a")
        s_hi = sem("s_hi")
        s_diag = sem("s_diag")
        s_rest = sem("s_rest")
        s_mid = sem("s_mid")
        s_lo = sem("s_lo")
        s_h_act = sem("s_h_act")
        s_h_dve = sem("s_h_dve")
        s_x2 = sem("s_x2")
        s_x2T = sem("s_x2T")
        s_y1 = sem("s_y1")
        s_y = sem("s_y")

        x_d = x.rearrange("(g t p) d -> g p t d", p=P, t=PER)
        out_d = out.rearrange("(g t p) d -> g p t d", p=P, t=PER)

        def tiles(buf, g):
            return buf[:, g, :].rearrange("p (t d) -> p t d", t=PER)

        def gate(layer, g):
            v = qe[:, layer, :, GB * g:GB * (g + 1)]
            return v.unsqueeze(3).to_broadcast([P, KD, GB, N])

        def by_batch(ap):
            return ap.rearrange("p (k b i) -> p k b i", k=KD, b=GB)

        def tile_of(buf, g, t):
            return buf[:, g, t * D:(t + 1) * D]

        def bias(n):
            v = half_b1[:, :] if n == 1 else b_sb[:, n, :]
            return v.unsqueeze(1).to_broadcast([P, PER, D])

        def by_tile(ap):
            return ap.rearrange("p (t d) -> p t d", t=PER)

        turn_end = [z_ps[0], z_ps[1]]
        lin_end = [z_ps[2], z_ps[3]]

        block = ctx.enter_context(nc.Block())

        @block.sync
        def _(sp):
            def weight(n):
                sp.dma_start(wl_sb[:, n, :, :], w_lin[n].rearrange("(k p) e -> p k e", p=P)).then_inc(s_wl[n], 16)

            sp.dma_start(q_sb[:, :], q_pack).then_inc(s_q, 16)
            weight(0)
            sp.dma_start(b_sb[:, :, :], biases.partition_broadcast(P)).then_inc(s_b, 16)
            sp.dma_start(w31_sb[:, :], w3_1).then_inc(s_w31, 16)
            weight(1)
            sp.dma_start(pick_sb[:, :, :], pick_m).then_inc(s_pick, 16)
            sp.dma_start(gather_sb[:, :, :], gather_m).then_inc(s_pick, 16)
            weight(2)
            for g in range(GROUPS):
                sp.wait_ge(s_lo, g + 1)
                for s in range(STRIPS):
                    sp.dma_start(a3[:, g, s, :], a_parts[s * N:(s + 1) * N, g, :, :]).then_inc(s_a3[g], 16)
            for g in range(LAST):
                sp.wait_ge(s_y, g + 1)
                sp.dma_start(out_d[g], tiles(y, g)).then_inc(s_out, 16)
            for t in range(PER):
                sp.wait_ge(s_y, LAST + t + 1)
                sp.dma_start(out_d[LAST][:, t, :], tile_of(y, LAST, t)).then_inc(s_out, 16)
            sp.wait_ge(s_out, 16 * (LAST + PER))

        @block.gpsimd
        def _(pool):
            nc.gpsimd.memset(warm_sb[:, :], 1.0).then_inc(s_warm, 1)

        @block.scalar
        def _(act):
            for g in range(GROUPS):
                act.dma_start(tiles(x_sb, g), x_d[g]).then_inc(s_x[g], 16)
                if g == 0:
                    act.dma_start(sq_sb[:, :, :], squares).then_inc(s_sq, 16)

            def step(name, g):
                if name == "lin1":
                    act.wait_ge(s_a, g + 1)
                    nc.scalar.copy(a_hi[:, g, :], a[:, g, :]).then_inc(s_hi, 1)
                    nc.scalar.activation(diag[:, g, :], a[:, g, :], ACT.Relu, scale=2.0).then_inc(s_diag, 1)
                if name == "turn2":
                    act.wait_ge(s_turn2, g + 1)
                    nc.scalar.copy(x2T[:, g, :], end_ps[:, :]).then_inc(s_x2T, 1)

            def quad(k):
                for s in range(STRIPS):
                    if on_scalar(k, s):
                        act.wait_ge(s_z, STRIPS * k + s + 1)
                        if k >= RING:
                            act.wait_ge(s_sum, k - RING + 1)
                        nc.scalar.activation(h[:, k % RING * STRIPS + s, :], z_ps[s][:, :],
                                             ACT.Relu).then_inc(s_h_act, 1)

            for st in LEAD:
                step(*st)
            quad(0)
            for k in range(QUADS):
                if k + 1 < QUADS:
                    quad(k + 1)
                for st in BETWEEN.get(k, []):
                    step(*st)
            for t in range(PER):
                act.wait_ge(s_turn2, LAST + t + 1)
                nc.scalar.copy(x2T[:, LAST, :].rearrange("p (k t d) -> p k t d", k=KD, t=PER)[:, :, t, :],
                               turn_end[t][:, 0:D].rearrange("p (k d) -> p k d", k=KD)).then_inc(s_x2T, 1)

        @block.vector
        def _(dve):
            def gates(layer, bank):
                b3 = q_sb[:, BATCHES + layer * KD:BATCHES + (layer + 1) * KD]
                dve.wait_ge(s_qe_ps, layer + 1)
                nc.vector.tensor_tensor(q_lin[:, layer, :, :],
                                        bank[:, 0:KD * BATCHES].rearrange("p (k b) -> p k b", k=KD),
                                        b3.unsqueeze(2).to_broadcast([P, KD, BATCHES]),
                                        ALU.add).then_inc(s_q_lin, 1)
                dve.wait_ge(s_q_lin, layer + 1)
                nc.vector.tensor_scalar(qe[:, layer, :, :], q_lin[:, layer, :, :], 0.0, None,
                                        ALU.max).then_inc(s_qe, 1)

            def step(name, g):
                if name == "mix":
                    dve.wait_ge(s_mixed, g + 1)
                    dve.wait_ge(s_qe, 1)
                    nc.vector.tensor_tensor(by_batch(zT[:, g, :]), by_batch(z_ps[g][:, :]), gate(0, g),
                                            ALU.mult).then_inc(s_zT, 1)
                if name == "lin0":
                    if g == 0:
                        dve.wait_ge(s_b, 16)
                    dve.wait_ge(s_lin0, g + 1)
                    nc.vector.tensor_tensor(by_tile(y0[:, g, :]), by_tile(end_ps[:, :]), bias(0),
                                            ALU.add).then_inc(s_y0, 1)
                    dve.wait_ge(s_y0, g + 1)
                    nc.vector.scalar_tensor_tensor(out=x1[:, g, :], in0=y0[:, g, :], scalar=0.0,
                                                   in1=x_sb[:, g, :], op0=ALU.max,
                                                   op1=ALU.add).then_inc(s_x1, 1)
                if name == "turn1":
                    dve.wait_ge(s_turn1, g + 1)
                    dve.wait_ge(s_qe, 2)
                    nc.vector.tensor_tensor(by_batch(uT[:, g, :]), by_batch(turn_ps[:, :]), gate(1, g),
                                            ALU.mult).then_inc(s_uT, 1)
                if name == "lin1":
                    dve.wait_ge(s_half, 1)
                    dve.wait_ge(s_lin1, g + 1)
                    nc.vector.tensor_tensor(by_tile(a[:, g, :]), by_tile(lin_ps[:, :]), bias(1),
                                            ALU.add).then_inc(s_a, 1)
                    dve.wait_ge(s_a, g + 1)
                    dve.wait_ge(s_hi, g + 1)
                    nc.vector.tensor_tensor(a_rest[:, g, :], a[:, g, :], a_hi[:, g, :],
                                            ALU.subtract).then_inc(s_rest, 1)
                    dve.wait_ge(s_rest, g + 1)
                    nc.vector.tensor_copy(a_mid[:, g, :], a_rest[:, g, :]).then_inc(s_mid, 1)
                    dve.wait_ge(s_mid, g + 1)
                    nc.vector.tensor_tensor(a_lo[:, g, :], a_rest[:, g, :], a_mid[:, g, :],
                                            ALU.subtract).then_inc(s_lo, 1)
                if name == "lin2":
                    dve.wait_ge(s_lin2, g + 1)
                    nc.vector.tensor_tensor(by_tile(y1[:, g, :]), by_tile(end_ps[:, :]), bias(2),
                                            ALU.add).then_inc(s_y1, 1)
                    dve.wait_ge(s_y1, g + 1)
                    nc.vector.scalar_tensor_tensor(out=y[:, g, :], in0=y1[:, g, :], scalar=0.0,
                                                   in1=x1[:, g, :], op0=ALU.max,
                                                   op1=ALU.add).then_inc(s_y, 1)

            def quad(k):
                for s in range(STRIPS):
                    if not on_scalar(k, s):
                        dve.wait_ge(s_z, STRIPS * k + s + 1)
                        if k >= RING:
                            dve.wait_ge(s_sum, k - RING + 1)
                        nc.vector.tensor_scalar(h[:, k % RING * STRIPS + s, :], z_ps[s][:, :], 0.0, None,
                                                ALU.max).then_inc(s_h_dve, 1)

            def add_diag(g):
                dve.wait_ge(s_sum, CHUNKS * (g + 1))
                dve.wait_ge(s_diag, g + 1)
                if g < LAST:
                    nc.vector.tensor_tensor(x2[:, g, :], sum_ps[:, :], diag[:, g, :], ALU.add).then_inc(s_x2, 1)
                else:
                    for t in range(PER):
                        nc.vector.tensor_tensor(tile_of(x2, g, t), sum_ps[:, t * D:(t + 1) * D],
                                                tile_of(diag, g, t), ALU.add).then_inc(s_x2, 1)

            gates(0, sum_ps)
            step("mix", 0)
            gates(1, turn_ps)
            for n, st in enumerate(LEAD):
                step(*st)
                if n == 1:
                    nc.vector.tensor_scalar(half_b1[:, :], b_sb[:, 1, :], 0.5, None, ALU.mult).then_inc(s_half, 1)
            quad(0)
            for k in range(QUADS):
                if k + 1 < QUADS:
                    quad(k + 1)
                for st in BETWEEN.get(k, []):
                    step(*st)
                if k % CHUNKS == CHUNKS - 1:
                    add_diag(k // CHUNKS)
            step("lin2", LAST - 1)
            for t in range(PER):
                dve.wait_ge(s_lin2, LAST + t + 1)
                nc.vector.tensor_tensor(tile_of(y1, LAST, t), lin_end[t][:, 0:D], b_sb[:, 2, :],
                                        ALU.add).then_inc(s_y1, 1)
                dve.wait_ge(s_y1, LAST + t + 1)
                nc.vector.scalar_tensor_tensor(out=tile_of(y, LAST, t), in0=tile_of(y1, LAST, t), scalar=0.0,
                                               in1=tile_of(x1, LAST, t), op0=ALU.max,
                                               op1=ALU.add).then_inc(s_y, 1)

        @block.tensor
        def _(pe):
            def product(out, lhs, n, g, t):
                for k in range(KD):
                    mm = nc.tensor.matmul(out, lhs[:, g, (k * PER + t) * P:(k * PER + t + 1) * P],
                                          wl_sb[:, n, k, :], start=(k == 0), stop=(k == KD - 1))
                return mm

            def products(bank, lhs, n, g):
                for t in range(PER):
                    mm = product(bank[:, t * D:(t + 1) * D], lhs, n, g, t)
                return mm

            def turn(bank, src, g, t, k, col):
                return nc.tensor.transpose(bank[:, col * P:(col + 1) * P],
                                           src[:, g, t * D + k * P:t * D + (k + 1) * P], sq_sb[:, 1, :])

            def turns(bank, src, g):
                for k in range(KD):
                    for t in range(PER):
                        mm = turn(bank, src, g, t, k, k * PER + t)
                return mm

            def step(name, g):
                if name == "mix":
                    pe.wait_ge(s_x[g], 16)
                    for k in range(KD):
                        for t in range(PER):
                            mm = nc.tensor.matmul(z_ps[g][:, (k * PER + t) * P:(k * PER + t + 1) * P],
                                                  x_sb[:, g, t * D + k * P:t * D + (k + 1) * P],
                                                  sq_sb[:, 0, :], start=True, stop=True)
                    mm.then_inc(s_mixed, 1)
                if name == "lin0":
                    if g == 0:
                        pe.wait_ge(s_wl[0], 16)
                    else:
                        pe.wait_ge(s_y0, g)
                    pe.wait_ge(s_zT, g + 1)
                    products(end_ps, zT, 0, g).then_inc(s_lin0, 1)
                if name == "turn1":
                    if g == 0:
                        pe.wait_ge(s_q_lin, 2)
                    else:
                        pe.wait_ge(s_uT, g)
                    pe.wait_ge(s_x1, g + 1)
                    turns(turn_ps, x1, g).then_inc(s_turn1, 1)
                if name == "lin1":
                    if g == 0:
                        pe.wait_ge(s_wl[1], 16)
                    else:
                        pe.wait_ge(s_a, g)
                    pe.wait_ge(s_uT, g + 1)
                    products(lin_ps, uT, 1, g).then_inc(s_lin1, 1)
                if name == "turn2":
                    if g == 0:
                        pe.wait_ge(s_y0, GROUPS)
                    else:
                        pe.wait_ge(s_y1, g)
                    pe.wait_ge(s_x2, g + 1)
                    turns(end_ps, x2, g).then_inc(s_turn2, 1)
                if name == "lin2":
                    if g == 0:
                        pe.wait_ge(s_wl[2], 16)
                    pe.wait_ge(s_x2T, g + 1)
                    products(end_ps, x2T, 2, g).then_inc(s_lin2, 1)

            def pair_sums(k):
                g, c = k // CHUNKS, k % CHUNKS
                if k == 0:
                    pe.wait_ge(s_pick, 32)
                    pe.wait_ge(s_zT, GROUPS)
                if c == 0:
                    pe.wait_ge(s_a3[g], 16 * STRIPS)
                for s in range(STRIPS):
                    if k >= 1:
                        who = on_scalar(k - 1, s)
                        pe.wait_ge(s_h_act if who else s_h_dve, relus(k - 1, s, who))
                    nc.tensor.matmul(z_ps[s][:, :], pick_sb[:, c, :], a3[:, g, s, :], start=True,
                                     stop=True).then_inc(s_z, 1)

            def sum_pairs(k):
                g, c = k // CHUNKS, k % CHUNKS
                if c == 0 and g == 0:
                    pe.wait_ge(s_q_lin, 1)
                if c == 0 and g >= 1:
                    pe.wait_ge(s_x2, g)
                for s in range(STRIPS):
                    who = on_scalar(k, s)
                    pe.wait_ge(s_h_act if who else s_h_dve, relus(k, s, who))
                    mm = nc.tensor.matmul(sum_ps[s * N:(s + 1) * N, :], gather_sb[:, c, :],
                                          h[:, k % RING * STRIPS + s, :], start=(c == 0),
                                          stop=(c == CHUNKS - 1))
                mm.then_inc(s_sum, 1)

            def gates(bank, w):
                for k in range(KD):
                    mm = nc.tensor.matmul(bank[:, k * BATCHES:(k + 1) * BATCHES], w[:, k * P:(k + 1) * P],
                                          q_sb[:, 0:BATCHES], start=True, stop=True)
                mm.then_inc(s_qe_ps, 1)

            pe.wait_ge(s_warm, 1)
            for _ in range(WARM):
                nc.tensor.matmul(lin_ps[:, :], warm_sb[:, 0:P], warm_sb[:, :], start=True, stop=True)
            pe.wait_ge(s_q, 16)
            gates(sum_ps, q_sb[:, BATCHES + 2 * KD:])
            pe.wait_ge(s_sq, 16)
            step("mix", 0)
            pe.wait_ge(s_w31, 16)
            gates(turn_ps, w31_sb)
            for st in LEAD:
                step(*st)
            pair_sums(0)
            for k in range(QUADS):
                if k + 1 < QUADS:
                    pair_sums(k + 1)
                for st in BETWEEN.get(k, []):
                    step(*st)
                sum_pairs(k)

            pe.wait_ge(s_x2T, LAST)
            product(end_ps[:, 0:D], x2T, 2, LAST - 1, 0)
            for t in range(PER):
                if t == 0:
                    pe.wait_ge(s_h_act, relus(QUADS - 1, STRIPS - 1, True))
                    pe.wait_ge(s_h_dve, relus(QUADS - 1, STRIPS - 1, False))
                pe.wait_ge(s_x2, LAST + t + 1)
                for k in range(KD):
                    mm = turn(turn_end[t], x2, LAST, t, k, k)
                mm.then_inc(s_turn2, 1)
            product(end_ps[:, D:2 * D], x2T, 2, LAST - 1, 1).then_inc(s_lin2, 1)
            for t in range(PER):
                pe.wait_ge(s_x2T, LAST + t + 1)
                product(lin_end[t][:, 0:D], x2T, 2, LAST, t).then_inc(s_lin2, 1)


def constants():
    import numpy as np

    mix = np.kron(np.eye(STRIPS), N * np.eye(N) + np.ones((N, N))).astype(np.float32)
    pairs = [(i, j) for i in range(N) for j in range(i + 1, N)]
    pick = np.zeros((K3, CHUNKS, P), mybir.dt.np(BF16))
    gather = np.zeros((P, CHUNKS, N), np.float32)
    for n, pair in enumerate(pairs):
        c, p = n // PC, n % PC
        for row in pair:
            pick[row * PARTS:(row + 1) * PARTS, c, p] = 1
            gather[p, c, row] = 1
    return np.stack([mix, np.eye(P, dtype=np.float32)], axis=1), pick, gather


def kernel(x, cond_1024, L0_cond_W3, L0_cond_b3, L0_cond_W2, L0_cond_b2, L1_cond_W1, L1_cond_b1,
           L1_cond_W2, L1_cond_b2, L1_cond_W3, L1_cond_b3):
    import numpy as np
    import concourse.bacc as bacc
    from concourse.bass_utils import run_bass_kernel_spmd

    squares, pick, gather = constants()
    b3 = np.stack([L0_cond_b3, L1_cond_b3]).reshape(2 * KD, P)
    arrays = {
        "x_in": np.ascontiguousarray(x).reshape(BATCHES * N, D),
        "q_pack_in": np.concatenate([np.asarray(cond_1024).T, b3.T, np.asarray(L0_cond_W3)], axis=1),
        "w3_1_in": np.ascontiguousarray(L1_cond_W3),
        "biases_in": np.stack([L0_cond_b2, L1_cond_b1, L1_cond_b2]),
        "w_lin_in": np.stack([L0_cond_W2, L1_cond_W1, L1_cond_W2]),
        "squares_in": squares,
        "pick_in": pick,
        "gather_in": gather,
    }
    nc = bacc.Bacc("TRN2", target_bir_lowering=False, num_devices=1)
    args = [nc.dram_tensor(name, a.shape, mybir.dt.from_np(a.dtype), kind="ExternalInput").ap()
            for name, a in arrays.items()]
    args.append(nc.dram_tensor("out", (BATCHES * N, D), F32, kind="ExternalOutput").ap())
    build(nc, *args)
    r = run_bass_kernel_spmd(nc, [arrays], core_ids=[0])
    return r.results[0]["out"].reshape(BATCHES, N, D)
```

```python
from contextlib import ExitStack

import concourse.bass as bass
from concourse import mybir

F32 = mybir.dt.float32
BF16 = mybir.dt.bfloat16
ALU = mybir.AluOpType
ACT = mybir.ActivationFunctionType

P = 128
BATCHES, N, D, Q = 32, 32, 256, 128
KD = D // P
STRIPS = P // N
TILES = BATCHES // STRIPS
PER = 2
GROUPS = TILES // PER
W = PER * D
GR = PER * P
GB = PER * STRIPS
CHUNKS = 4
PAIRS = N * (N - 1) // 2
PC = PAIRS // CHUNKS
PARTS = 3
K3 = PARTS * N
QUADS = GROUPS * CHUNKS
RING = 2
WARM = 10

LEAD_TENSOR = [("lin0", 0), ("lin0", 1), ("lin1", 0), ("lin0", 2), ("lin1", 1), ("lin0", 3), ("lin1", 2)]
LEAD_SCALAR = [("lin0", 0), ("lin0", 1), ("hi", 0), ("mid", 0), ("lin0", 2), ("diag", 0), ("hi", 1),
               ("lin0", 3), ("diag", 1)]
LEAD_VECTOR = [("sum", 0), ("mix", 0), ("gate", 0), ("z", 0), ("sum", 1), ("mix", 1), ("z", 1), ("gate", 1),
               ("sum", 2), ("lin0", 0), ("u", 0), ("mix", 2), ("lin0", 1), ("u", 1), ("sum", 3), ("half", 0),
               ("lin1", 0), ("mix", 3), ("rest", 0), ("lo", 0), ("lin0", 2), ("lin1", 1),
               ("lin0", 3), ("u", 3), ("lin1", 2)]
LEAD_POOL = [("z", 2), ("z", 3), ("u", 2)]
SECOND = [("lin1", 3)]
BETWEEN = {5: [("turn2", 0)], 6: [("lin2", 0)], 9: [("turn2", 1)], 10: [("lin2", 1)], 13: [("turn2", 2)]}
BETWEEN_SCALAR = {0: [("hi", 2)], 1: [("diag", 2), ("hi", 3)], 2: [("diag", 3)], **BETWEEN}
LAST = GROUPS - 1


def on_scalar(k, s):
    return s != 3


def relus(k, s, scalar):
    return sum(on_scalar(kk, ss) == scalar for kk in range(k + 1) for ss in range(STRIPS)
               if kk < k or ss <= s)


def build(nc, xT, q_pack, b1, w_lin, ident_m, pick_m, gather_m, outT):
    ctx = ExitStack()
    with ctx:
        def sb(name, shape, dt=F32):
            return ctx.enter_context(nc.sbuf_tensor(name, shape, dt))

        def bank(name):
            return ctx.enter_context(nc.psum_tensor(name, [P, W], F32))

        def sem(name):
            return ctx.enter_context(nc.semaphore(name))

        x_sb = sb("x_sb", [P, GROUPS, W])
        q_sb = sb("q_sb", [Q, BATCHES + 4 * KD + 2 * D])
        wl_sb = sb("wl_sb", [P, 3, KD, D])
        b1_sb = sb("b1_sb", [P, D])
        half_b1 = sb("half_b1", [P, D])
        id_sb = sb("id_sb", [P, P])
        warm_sb = sb("warm_sb", [P, W], BF16)
        pick_sb = sb("pick_sb", [K3, CHUNKS, P], BF16)
        gather_sb = sb("gather_sb", [P, CHUNKS, N])
        qe = sb("qe", [P, 2, KD, BATCHES])
        q_lin = sb("q_lin", [P, 2, KD, BATCHES])
        x_sum = sb("x_sum", [P, GROUPS, KD * GB])
        x_mix = sb("x_mix", [P, GROUPS, W])
        zT = sb("zT", [P, GROUPS, W])
        r0 = sb("r0", [P, GROUPS, W])
        x1 = sb("x1", [P, GROUPS, W])
        uT = sb("uT", [P, GROUPS, W])
        a = sb("a", [P, GROUPS, W])
        a_parts = sb("a_parts", [P, GROUPS, PARTS, W], BF16)
        a_hi, a_mid, a_lo = (a_parts[:, :, part, :] for part in range(PARTS))
        a_rest = sb("a_rest", [P, GROUPS, W])
        diag = sb("diag", [P, GROUPS, W])
        a3 = sb("a3", [K3, GROUPS, STRIPS, W], BF16)
        h = sb("h", [P, RING * STRIPS, W])
        x2 = sb("x2", [P, GROUPS, W])
        x2T = sb("x2T", [P, GROUPS, W])
        r1 = sb("r1", [P, GROUPS, W])
        y = sb("y", [P, GROUPS, W])

        z_ps = [bank(f"z_ps{s}") for s in range(STRIPS)]
        sum_ps = bank("sum_ps")
        turn_ps = bank("turn_ps")
        lin_ps = bank("lin_ps")
        end_ps = bank("end_ps")

        s_x = [sem(f"s_x_in{g}") for g in range(GROUPS)]
        s_q = sem("s_q")
        s_id = sem("s_id")
        s_wl = [sem(f"s_wl{n}") for n in range(3)]
        s_b = sem("s_b")
        s_pick = sem("s_pick")
        s_a3 = [[sem(f"s_a3_{g}{s}") for s in range(STRIPS)] for g in range(GROUPS)]
        s_out = sem("s_out")
        s_warm = sem("s_warm")
        s_qe_ps = sem("s_qe_ps")
        s_lin0 = sem("s_lin0")
        s_lin1 = sem("s_lin1")
        s_z = sem("s_z")
        s_sum = sem("s_sum")
        s_turn2 = sem("s_turn2")
        s_lin2 = sem("s_lin2")
        s_q_lin = sem("s_q_lin")
        s_qe = sem("s_qe")
        s_x_sum = sem("s_x_sum")
        s_x_mix = sem("s_x_mix")
        s_zT = sem("s_zT")
        s_zT_pool = sem("s_zT_pool")
        s_half = sem("s_half")
        s_r0 = sem("s_r0")
        s_x1 = sem("s_x1")
        s_uT = sem("s_uT")
        s_uT_pool = sem("s_uT_pool")
        s_a = sem("s_a")
        s_hi = sem("s_hi")
        s_diag = sem("s_diag")
        s_rest = sem("s_rest")
        s_mid = sem("s_mid")
        s_lo = sem("s_lo")
        s_h_act = sem("s_h_act")
        s_h_dve = sem("s_h_dve")
        s_x2 = sem("s_x2")
        s_x2T = sem("s_x2T")
        s_r1 = sem("s_r1")
        s_y = sem("s_y")

        def gate(layer, g):
            v = qe[:, layer, :, GB * g:GB * (g + 1)]
            return v.unsqueeze(3).to_broadcast([P, KD, GB, N])

        def by_batch(ap):
            return ap.rearrange("p (k b i) -> p k b i", k=KD, b=GB)

        def tile_of(buf, g, t):
            return buf[:, g, t * D:(t + 1) * D]

        def rows_of(buf, g, t):
            return buf[:, g, :].rearrange("p (k r) -> p k r", k=KD)[:, :, t * P:(t + 1) * P]

        def by_half(ap):
            return ap.rearrange("p (k r) -> p k r", k=KD)

        def b2(layer, k):
            at = BATCHES + 2 * KD + layer * KD + k
            return q_sb[:, at:at + 1]

        def lin0_ps(g):
            return end_ps if g % 2 == 0 else turn_ps

        def lin1_ps(g):
            return lin_ps if g % 2 == 0 else (sum_ps if g == 1 else end_ps)

        turn_end = [z_ps[0], z_ps[1]]
        lin_end = [z_ps[2], z_ps[3]]

        block = ctx.enter_context(nc.Block())

        @block.sync
        def _(sp):
            def weight(n):
                sp.dma_start(wl_sb[:, n, :, :], w_lin[n].rearrange("(k p) e -> p k e", p=P)).then_inc(s_wl[n], 16)

            sp.dma_start(q_sb[:, :], q_pack).then_inc(s_q, 16)
            weight(0)
            sp.dma_start(b1_sb[:, :], b1.partition_broadcast(P)).then_inc(s_b, 16)
            weight(1)
            sp.dma_start(pick_sb[:, :, :], pick_m).then_inc(s_pick, 16)
            sp.dma_start(gather_sb[:, :, :], gather_m).then_inc(s_pick, 16)
            sp.dma_start(id_sb[:, :], ident_m).then_inc(s_id, 16)
            weight(2)
            for g in range(GROUPS):
                sp.wait_ge(s_lo, g + 1)
                for s in range(STRIPS):
                    sp.dma_start(a3[:, g, s, :], a_parts[s * N:(s + 1) * N, g, :, :]).then_inc(s_a3[g][s], 16)
            for g in range(LAST):
                sp.wait_ge(s_y, g + 1)
                sp.dma_start(outT[:, g, :], y[:, g, :]).then_inc(s_out, 16)
            for t in range(PER):
                sp.wait_ge(s_y, LAST + t + 1)
                sp.dma_start(outT[:, LAST, :].rearrange("p (k r) -> p k r", k=KD)[:, :, t * P:(t + 1) * P],
                             rows_of(y, LAST, t)).then_inc(s_out, 16)
            sp.wait_ge(s_out, 16 * (LAST + PER))

        @block.gpsimd
        def _(pool):
            nc.gpsimd.memset(warm_sb[:, :], 1.0).then_inc(s_warm, 1)
            for name, g in LEAD_POOL:
                if name == "z":
                    pool.wait_ge(s_x_mix, g + 1)
                    pool.wait_ge(s_qe, 1)
                    nc.gpsimd.tensor_tensor(by_batch(zT[:, g, :]), by_batch(x_mix[:, g, :]), gate(0, g),
                                            ALU.mult).then_inc(s_zT_pool, 1)
                if name == "u":
                    pool.wait_ge(s_x1, g + 1)
                    pool.wait_ge(s_qe, 2)
                    nc.gpsimd.tensor_tensor(by_batch(uT[:, g, :]), by_batch(x1[:, g, :]), gate(1, g),
                                            ALU.mult).then_inc(s_uT_pool, 1)
            for g in range(1, GROUPS):
                pool.wait_ge(s_hi, g + 1)
                nc.gpsimd.tensor_tensor(a_rest[:, g, :], a[:, g, :], a_hi[:, g, :],
                                        ALU.subtract).then_inc(s_rest, 1)
                pool.wait_ge(s_rest, g + 1)
                nc.gpsimd.tensor_copy(a_mid[:, g, :], a_rest[:, g, :]).then_inc(s_mid, 1)
                pool.wait_ge(s_mid, g + 1)
                nc.gpsimd.tensor_tensor(a_lo[:, g, :], a_rest[:, g, :], a_mid[:, g, :],
                                        ALU.subtract).then_inc(s_lo, 1)

        @block.scalar
        def _(act):
            for g in range(GROUPS):
                act.dma_start(x_sb[:, g, :], xT[:, g, :]).then_inc(s_x[g], 16)

            def step(name, g):
                if name == "lin0":
                    act.wait_ge(s_lin0, g + 1)
                    for k in range(KD):
                        last = nc.scalar.activation(r0[:, g, k * GR:(k + 1) * GR],
                                                    lin0_ps(g)[:, k * GR:(k + 1) * GR], ACT.Relu, bias=b2(0, k))
                    last.then_inc(s_r0, 1)
                if name == "hi":
                    act.wait_ge(s_a, g + 1)
                    nc.scalar.copy(a_hi[:, g, :], a[:, g, :]).then_inc(s_hi, 1)
                if name == "mid":
                    act.wait_ge(s_rest, g + 1)
                    nc.scalar.copy(a_mid[:, g, :], a_rest[:, g, :]).then_inc(s_mid, 1)
                if name == "diag":
                    act.wait_ge(s_a, g + 1)
                    nc.scalar.activation(diag[:, g, :], a[:, g, :], ACT.Relu, scale=2.0).then_inc(s_diag, 1)
                if name == "turn2":
                    act.wait_ge(s_turn2, g + 1)
                    nc.scalar.copy(x2T[:, g, :], turn_ps[:, :]).then_inc(s_x2T, 1)
                if name == "lin2":
                    act.wait_ge(s_lin2, g + 1)
                    for k in range(KD):
                        last = nc.scalar.activation(r1[:, g, k * GR:(k + 1) * GR], end_ps[:, k * GR:(k + 1) * GR],
                                                    ACT.Relu, bias=b2(1, k))
                    last.then_inc(s_r1, 1)

            def quad(k):
                for s in range(STRIPS):
                    if on_scalar(k, s):
                        act.wait_ge(s_z, STRIPS * k + s + 1)
                        if k >= RING:
                            act.wait_ge(s_sum, k - RING + 1)
                        nc.scalar.activation(h[:, k % RING * STRIPS + s, :], z_ps[s][:, :],
                                             ACT.Relu).then_inc(s_h_act, 1)

            for st in LEAD_SCALAR:
                step(*st)
            quad(0)
            for k in range(QUADS):
                if k + 1 < QUADS:
                    quad(k + 1)
                for st in BETWEEN_SCALAR.get(k, []):
                    step(*st)
            for t in range(PER):
                act.wait_ge(s_turn2, LAST + t + 1)
                nc.scalar.copy(rows_of(x2T, LAST, t), by_half(turn_end[t][:, 0:D])).then_inc(s_x2T, 1)
            step("lin2", LAST - 1)
            for t in range(PER):
                act.wait_ge(s_lin2, LAST + t + 1)
                for k in range(KD):
                    last = nc.scalar.activation(rows_of(r1, LAST, t)[:, k, :], lin_end[t][:, k * P:(k + 1) * P],
                                                ACT.Relu, bias=b2(1, k))
                last.then_inc(s_r1, 1)

        @block.vector
        def _(dve):
            def gates(layer, bank):
                b3 = q_sb[:, BATCHES + layer * KD:BATCHES + (layer + 1) * KD]
                dve.wait_ge(s_qe_ps, layer + 1)
                nc.vector.tensor_tensor(q_lin[:, layer, :, :],
                                        by_half(bank[:, 0:KD * P])[:, :, 0:BATCHES],
                                        b3.unsqueeze(2).to_broadcast([P, KD, BATCHES]),
                                        ALU.add).then_inc(s_q_lin, 1)
                dve.wait_ge(s_q_lin, layer + 1)
                nc.vector.tensor_scalar(qe[:, layer, :, :], q_lin[:, layer, :, :], 0.0, None,
                                        ALU.max).then_inc(s_qe, 1)

            def step(name, g):
                if name == "sum":
                    dve.wait_ge(s_x[g], 16)
                    nc.vector.tensor_reduce(x_sum[:, g, :], x_sb[:, g, :].rearrange("p (m i) -> p m i", i=N),
                                            mybir.AxisListType.X, ALU.add).then_inc(s_x_sum, 1)
                if name == "mix":
                    dve.wait_ge(s_x_sum, g + 1)
                    nc.vector.scalar_tensor_tensor(
                        out=x_mix[:, g, :].rearrange("p (m i) -> p m i", i=N),
                        in0=x_sb[:, g, :].rearrange("p (m i) -> p m i", i=N), scalar=float(N),
                        in1=x_sum[:, g, :].unsqueeze(2).to_broadcast([P, KD * GB, N]), op0=ALU.mult,
                        op1=ALU.add).then_inc(s_x_mix, 1)
                if name == "z":
                    dve.wait_ge(s_x_mix, g + 1)
                    dve.wait_ge(s_qe, 1)
                    nc.vector.tensor_tensor(by_batch(zT[:, g, :]), by_batch(x_mix[:, g, :]), gate(0, g),
                                            ALU.mult).then_inc(s_zT, 1)
                if name == "gate":
                    gates(g, (sum_ps, lin_ps)[g])
                if name == "lin0":
                    dve.wait_ge(s_r0, g + 1)
                    nc.vector.tensor_tensor(x1[:, g, :], r0[:, g, :], x_sb[:, g, :], ALU.add).then_inc(s_x1, 1)
                if name == "half":
                    dve.wait_ge(s_b, 16)
                    nc.vector.tensor_scalar(half_b1[:, :], b1_sb[:, :], 0.5, None, ALU.mult).then_inc(s_half, 1)
                if name == "u":
                    dve.wait_ge(s_x1, g + 1)
                    dve.wait_ge(s_qe, 2)
                    nc.vector.tensor_tensor(by_batch(uT[:, g, :]), by_batch(x1[:, g, :]), gate(1, g),
                                            ALU.mult).then_inc(s_uT, 1)
                if name == "lin1":
                    dve.wait_ge(s_half, 1)
                    dve.wait_ge(s_lin1, g + 1)
                    nc.vector.tensor_tensor(a[:, g, :].rearrange("p (t d) -> p t d", t=PER),
                                            lin1_ps(g)[:, :].rearrange("p (t d) -> p t d", t=PER),
                                            half_b1[:, :].unsqueeze(1).to_broadcast([P, PER, D]),
                                            ALU.add).then_inc(s_a, 1)
                if name == "rest":
                    dve.wait_ge(s_a, g + 1)
                    dve.wait_ge(s_hi, g + 1)
                    nc.vector.tensor_tensor(a_rest[:, g, :], a[:, g, :], a_hi[:, g, :],
                                            ALU.subtract).then_inc(s_rest, 1)
                if name == "lo":
                    dve.wait_ge(s_rest, g + 1)
                    dve.wait_ge(s_mid, g + 1)
                    nc.vector.tensor_tensor(a_lo[:, g, :], a_rest[:, g, :], a_mid[:, g, :],
                                            ALU.subtract).then_inc(s_lo, 1)
                if name == "lin2":
                    dve.wait_ge(s_r1, g + 1)
                    nc.vector.tensor_tensor(y[:, g, :], r1[:, g, :], x1[:, g, :], ALU.add).then_inc(s_y, 1)

            def quad(k):
                for s in range(STRIPS):
                    if not on_scalar(k, s):
                        dve.wait_ge(s_z, STRIPS * k + s + 1)
                        if k >= RING:
                            dve.wait_ge(s_sum, k - RING + 1)
                        nc.vector.tensor_scalar(h[:, k % RING * STRIPS + s, :], z_ps[s][:, :], 0.0, None,
                                                ALU.max).then_inc(s_h_dve, 1)

            def add_diag(g):
                dve.wait_ge(s_sum, CHUNKS * (g + 1))
                dve.wait_ge(s_diag, g + 1)
                if g < LAST:
                    nc.vector.tensor_tensor(x2[:, g, :], sum_ps[:, :], diag[:, g, :], ALU.add).then_inc(s_x2, 1)
                else:
                    for t in range(PER):
                        nc.vector.tensor_tensor(tile_of(x2, g, t), sum_ps[:, t * D:(t + 1) * D],
                                                tile_of(diag, g, t), ALU.add).then_inc(s_x2, 1)

            for st in LEAD_VECTOR:
                step(*st)
            quad(0)
            for st in SECOND:
                step(*st)
            for k in range(QUADS):
                if k + 1 < QUADS:
                    quad(k + 1)
                for st in BETWEEN.get(k, []):
                    step(*st)
                if k % CHUNKS == CHUNKS - 1:
                    add_diag(k // CHUNKS)
            step("lin2", LAST - 1)
            for t in range(PER):
                dve.wait_ge(s_r1, LAST + t + 1)
                nc.vector.tensor_tensor(rows_of(y, LAST, t), rows_of(r1, LAST, t), rows_of(x1, LAST, t),
                                        ALU.add).then_inc(s_y, 1)

        @block.tensor
        def _(pe):
            def to_features(out, rhs, n, half, parts=range(KD)):
                for k in parts:
                    mm = nc.tensor.matmul(out, wl_sb[:, n, k, half * P:(half + 1) * P], rhs[:, k, :],
                                          start=(k == 0), stop=(k == KD - 1))
                return mm

            def to_rows(out, lhs, n, g, t):
                for k in range(KD):
                    mm = nc.tensor.matmul(out, lhs[:, g, (k * PER + t) * P:(k * PER + t + 1) * P],
                                          wl_sb[:, n, k, :], start=(k == 0), stop=(k == KD - 1))
                return mm

            def features(bank, src, n, g):
                for half in range(KD):
                    mm = to_features(bank[:, half * GR:(half + 1) * GR], by_half(src[:, g, :]), n, half)
                return mm

            def turn(bank, src, g, t, k, col):
                return nc.tensor.transpose(bank[:, col * P:(col + 1) * P],
                                           src[:, g, t * D + k * P:t * D + (k + 1) * P], id_sb[:, :])

            def turns(bank, src, g):
                for k in range(KD):
                    for t in range(PER):
                        mm = turn(bank, src, g, t, k, k * PER + t)
                return mm

            def step(name, g):
                if name == "lin0":
                    if g == 0:
                        pe.wait_ge(s_wl[0], 16)
                    if g >= 2:
                        pe.wait_ge(s_r0, g - 1)
                    if g < 2:
                        pe.wait_ge(s_zT, g + 1)
                    else:
                        pe.wait_ge(s_zT_pool, g - 1)
                    features(lin0_ps(g), zT, 0, g).then_inc(s_lin0, 1)
                if name == "lin1":
                    if g == 0:
                        pe.wait_ge(s_wl[1], 16)
                        pe.wait_ge(s_q_lin, 2)
                    if g == 2:
                        pe.wait_ge(s_a, 1)
                    if g == 3:
                        pe.wait_ge(s_r0, 3)
                    if g == 2:
                        pe.wait_ge(s_uT_pool, 1)
                    else:
                        pe.wait_ge(s_uT, g + (g < 2))
                    for t in range(PER):
                        mm = to_rows(lin1_ps(g)[:, t * D:(t + 1) * D], uT, 1, g, t)
                    mm.then_inc(s_lin1, 1)
                if name == "turn2":
                    if g == 0:
                        pe.wait_ge(s_id, 16)
                        pe.wait_ge(s_r0, GROUPS)
                    else:
                        pe.wait_ge(s_x2T, g)
                    pe.wait_ge(s_x2, g + 1)
                    turns(turn_ps, x2, g).then_inc(s_turn2, 1)
                if name == "lin2":
                    if g == 0:
                        pe.wait_ge(s_wl[2], 16)
                        pe.wait_ge(s_a, GROUPS)
                    else:
                        pe.wait_ge(s_r1, g)
                    pe.wait_ge(s_x2T, g + 1)
                    features(end_ps, x2T, 2, g).then_inc(s_lin2, 1)

            def pair_sums(k):
                g, c = k // CHUNKS, k % CHUNKS
                if k == 0:
                    pe.wait_ge(s_pick, 32)
                for s in range(STRIPS):
                    if c == 0:
                        pe.wait_ge(s_a3[g][s], 16)
                    if k >= 1:
                        who = on_scalar(k - 1, s)
                        pe.wait_ge(s_h_act if who else s_h_dve, relus(k - 1, s, who))
                    nc.tensor.matmul(z_ps[s][:, :], pick_sb[:, c, :], a3[:, g, s, :], start=True,
                                     stop=True).then_inc(s_z, 1)

            def sum_pairs(k):
                g, c = k // CHUNKS, k % CHUNKS
                if c == 0 and g == 0:
                    pe.wait_ge(s_a, 2)
                if c == 0 and g >= 1:
                    pe.wait_ge(s_x2, g)
                for s in range(STRIPS):
                    who = on_scalar(k, s)
                    pe.wait_ge(s_h_act if who else s_h_dve, relus(k, s, who))
                    mm = nc.tensor.matmul(sum_ps[s * N:(s + 1) * N, :], gather_sb[:, c, :],
                                          h[:, k % RING * STRIPS + s, :], start=(c == 0),
                                          stop=(c == CHUNKS - 1))
                mm.then_inc(s_sum, 1)

            def gates(bank, w):
                q_wide = q_sb[:, 0:BATCHES].unsqueeze(1).to_broadcast([Q, P // BATCHES, BATCHES])
                for k in range(KD):
                    mm = nc.tensor.matmul(bank[:, k * P:(k + 1) * P], w[:, k * P:(k + 1) * P], q_wide,
                                          start=True, stop=True)
                mm.then_inc(s_qe_ps, 1)

            pe.wait_ge(s_warm, 1)
            for _ in range(WARM):
                nc.tensor.matmul(end_ps[:, :], warm_sb[:, 0:P], warm_sb[:, :], start=True, stop=True)
            pe.wait_ge(s_q, 16)
            gates(sum_ps, q_sb[:, BATCHES + 4 * KD:])
            gates(lin_ps, q_sb[:, BATCHES + 4 * KD + D:])
            for _ in range(WARM // 5):
                nc.tensor.matmul(end_ps[:, :], warm_sb[:, 0:P], warm_sb[:, :], start=True, stop=True)
            for st in LEAD_TENSOR:
                step(*st)
            pair_sums(0)
            for st in SECOND:
                step(*st)
            for k in range(QUADS):
                if k + 1 < QUADS:
                    pair_sums(k + 1)
                for st in BETWEEN.get(k, []):
                    step(*st)
                if k == QUADS - 2:
                    pe.wait_ge(s_x2T, LAST)
                    pe.wait_ge(s_r1, LAST - 1)
                    to_features(end_ps[:, 0:GR], by_half(x2T[:, LAST - 1, :]), 2, 0)
                sum_pairs(k)

            to_features(end_ps[:, GR:2 * GR], by_half(x2T[:, LAST - 1, :]), 2, 1, [0])
            pe.wait_ge(s_h_act, relus(QUADS - 1, STRIPS - 1, True))
            pe.wait_ge(s_h_dve, relus(QUADS - 1, STRIPS - 1, False))
            for t in range(PER):
                pe.wait_ge(s_x2, LAST + t + 1)
                for k in range(KD):
                    mm = turn(turn_end[t], x2, LAST, t, k, k)
                mm.then_inc(s_turn2, 1)
            to_features(end_ps[:, GR:2 * GR], by_half(x2T[:, LAST - 1, :]), 2, 1, [1]).then_inc(s_lin2, 1)
            for t in range(PER):
                pe.wait_ge(s_x2T, LAST + t + 1)
                for half in range(KD):
                    mm = to_features(lin_end[t][:, half * P:(half + 1) * P], rows_of(x2T, LAST, t), 2, half)
                mm.then_inc(s_lin2, 1)


def constants():
    import numpy as np

    pairs = [(i, j) for i in range(N) for j in range(i + 1, N)]
    pick = np.zeros((K3, CHUNKS, P), mybir.dt.np(BF16))
    gather = np.zeros((P, CHUNKS, N), np.float32)
    for n, pair in enumerate(pairs):
        c, p = n // PC, n % PC
        for row in pair:
            pick[row * PARTS:(row + 1) * PARTS, c, p] = 1
            gather[p, c, row] = 1
    return np.eye(P, dtype=np.float32), pick, gather


def kernel(x, cond_1024, L0_cond_W3, L0_cond_b3, L0_cond_W2, L0_cond_b2, L1_cond_W1, L1_cond_b1,
           L1_cond_W2, L1_cond_b2, L1_cond_W3, L1_cond_b3):
    import numpy as np
    import concourse.bacc as bacc
    from concourse.bass_utils import run_bass_kernel_spmd

    ident, pick, gather = constants()
    columns = np.concatenate([L0_cond_b3, L1_cond_b3, L0_cond_b2, L1_cond_b2]).reshape(4 * KD, P).T
    x_groups = np.asarray(x).reshape(GROUPS, GR, KD, P)
    arrays = {
        "xT_in": np.ascontiguousarray(x_groups.transpose(3, 0, 2, 1)).reshape(P, GROUPS, W),
        "q_pack_in": np.concatenate([np.asarray(cond_1024).T, columns, np.asarray(L0_cond_W3),
                                     np.asarray(L1_cond_W3)], axis=1),
        "b1_in": np.ascontiguousarray(L1_cond_b1),
        "w_lin_in": np.stack([L0_cond_W2, L1_cond_W1, L1_cond_W2]),
        "ident_in": ident,
        "pick_in": pick,
        "gather_in": gather,
    }
    nc = bacc.Bacc("TRN2", target_bir_lowering=False, num_devices=1)
    args = [nc.dram_tensor(name, a.shape, mybir.dt.from_np(a.dtype), kind="ExternalInput").ap()
            for name, a in arrays.items()]
    args.append(nc.dram_tensor("outT", (P, GROUPS, W), F32, kind="ExternalOutput").ap())
    build(nc, *args)
    r = run_bass_kernel_spmd(nc, [arrays], core_ids=[0])
    groups = r.results[0]["outT"].reshape(P, GROUPS, KD, GR)
    return np.ascontiguousarray(groups.transpose(1, 3, 2, 0)).reshape(BATCHES, N, D)
```

```python
from contextlib import ExitStack

import concourse.bass as bass
from concourse import mybir

F32 = mybir.dt.float32
BF16 = mybir.dt.bfloat16
ALU = mybir.AluOpType
ACT = mybir.ActivationFunctionType

P = 128
BATCHES, N, D, Q = 32, 32, 256, 128
KD = D // P
STRIPS = P // N
TILES = BATCHES // STRIPS
PER = 2
GROUPS = TILES // PER
W = PER * D
GR = PER * P
GB = PER * STRIPS
CHUNKS = 4
PAIRS = N * (N - 1) // 2
PC = PAIRS // CHUNKS
PARTS = 3
K3 = PARTS * N
OWN = 0
PAIRED = [g for g in range(GROUPS) if g != OWN]
QUADS = len(PAIRED) * CHUNKS
RING = 2
UNITS = KD * GB
SLOTS = 8
Q0 = BATCHES + 5 * KD + D

TENSOR_LEAD = [("warm", 2), ("gate", 0), ("warm", 3), ("gate", 1), ("lin0", 0), ("lin0", 1),
               ("lin1", 0), ("lin0", 2), ("lin1", 1), ("lin0", 3), ("lin1", 2), ("lin1", 3)]
TENSOR = {5: [("turn2", 1)], 8: [("lin2", 1)], 9: [("turn2", 2)], 10: [("lin2", 2)]}
TENSOR_TAIL = [("own", 0), ("turn_end", 0), ("own", 1), ("turn_end", 1), ("lin_end", 0), ("own", 2),
               ("own", 3), ("lin_end", 1)]
SCALAR_LEAD = [("lin0", 0), ("lin0", 1), ("aT", 0), ("lin0", 2), ("relu", 0), ("hi", 1), ("diag", 1),
               ("lin0", 3), ("mid", 1), ("relu", 1), ("relu", 2), ("hi", 2), ("relu", 3)]
SCALAR = {-1: [("relu", 4), ("mid", 2)], 0: [("relu", 5)], 1: [("hi", 3), ("relu", 6)],
          3: [("diag", 2), ("relu", 7)], 4: [("relu", 8)], 5: [("relu", 9)],
          7: [("turn2", 1), ("relu", 10), ("relu", 11)], 8: [("lin2", 1)],
          9: [("relu", 12), ("turn2", 2), ("relu", 13), ("relu", 14)],
          11: [("relu", 15), ("lin2", 2), ("turn_end", 0), ("turn_end", 1)]}
SCALAR_TAIL = [("lin_end", 0), ("own", 0), ("own", 1), ("lin_end", 1)]
VECTOR_LEAD = [("sum", 0), ("gate", 0), ("mix", 0), ("sum", 1), ("sum", 2), ("mix", 1), ("mix", 2),
               ("gate", 1), ("x1", 0), ("u", 0), ("sum", 3), ("half", 0), ("mix", 3), ("u", 1),
               ("x1", 2), ("a", 1), ("add_up", 0), ("rest", 1), ("x1", 3), ("lo", 1), ("u", 3),
               ("a", 2), ("add_up", 1), ("rest", 2), ("add_up", 2)]
VECTOR = {0: [("add_up", 3)], 1: [("a", 3), ("add_up", 4)], 2: [("add_up", 5), ("mid", 3)], 3: [("x2", 1)],
          4: [("add_up", 6)], 5: [("add_up", 7)], 6: [("add_up", 8)], 7: [("add_up", 9), ("x2", 2)],
          8: [("add_up", 10), ("add_up", 11)], 9: [("add_up", 12)], 10: [("diag", 3)],
          11: [("add_up", 13), ("add_up", 14), ("x2", 3), ("add_up", 15), ("y", 1), ("y_end", 0)]}
VECTOR_TAIL = [("y_own", 0), ("y_end", 1)]
POOL = [("z", 0), ("z", 1), ("z", 2), ("x1", 1), ("z", 3), ("pair", 0), ("u", 2), ("pair", 1),
        ("pair", 2), ("pair", 3), ("pair", 4), ("pair", 5), ("lo", 2), ("pair", 6), ("pair", 7),
        ("rest", 3), ("pair", 8), ("lo", 3), ("pair", 9), ("pair", 10), ("pair", 11), ("pair", 12),
        ("pair", 13), ("pair", 14), ("pair", 15), ("y", 2)]
ON_VECTOR = [(2, 3), (0, 2), (1,), (0, 2), (2,), (0, 3), (1,), (0, 2), (2,), (1,), (0, 1, 3), (1,)]
LAST = GROUPS - 1


def nth(g):
    return PAIRED.index(g) + 1


def on_scalar(k, s):
    return s not in ON_VECTOR[k]


def relus(k, s, scalar):
    return sum(on_scalar(kk, ss) == scalar for kk in range(k + 1) for ss in range(STRIPS)
               if kk < k or ss <= s)


def build(nc, xT, q_pack, b1, w_lin, ident_m, pick_m, gather_m, outT):
    ctx = ExitStack()
    with ctx:
        def sb(name, shape, dt=F32):
            return ctx.enter_context(nc.sbuf_tensor(name, shape, dt))

        def bank(name):
            return ctx.enter_context(nc.psum_tensor(name, [P, W], F32))

        def sem(name):
            return ctx.enter_context(nc.semaphore(name))

        x_sb = sb("x_sb", [P, GROUPS, W])
        q_sb = sb("q_sb", [Q, BATCHES + 5 * KD + 2 * D])
        wl_sb = sb("wl_sb", [P, 3, KD, D])
        b1_sb = sb("b1_sb", [P, D])
        half_b1 = sb("half_b1", [P, D])
        id_sb = sb("id_sb", [P, P])
        half_b1c = sb("half_b1c", [P, KD])
        aT = sb("aT", [P, W])
        pairs = sb("pairs", [P, SLOTS, N, N])
        warm_sb = sb("warm_sb", [P, W], BF16)
        pick_sb = sb("pick_sb", [K3, CHUNKS, P], BF16)
        gather_sb = sb("gather_sb", [P, CHUNKS, N])
        qe = sb("qe", [P, 2, KD, BATCHES])
        q_lin = sb("q_lin", [P, 2, KD, BATCHES])
        x_sum = sb("x_sum", [P, GROUPS, KD * GB])
        x_mix = sb("x_mix", [P, GROUPS, W])
        zT = sb("zT", [P, GROUPS, W])
        r0 = sb("r0", [P, GROUPS, W])
        x1 = sb("x1", [P, GROUPS, W])
        uT = sb("uT", [P, GROUPS, W])
        a = sb("a", [P, GROUPS, W])
        a_parts = sb("a_parts", [P, GROUPS, PARTS, W], BF16)
        a_hi, a_mid, a_lo = (a_parts[:, :, part, :] for part in range(PARTS))
        a_rest = sb("a_rest", [P, GROUPS, W])
        diag = sb("diag", [P, GROUPS, W])
        a3 = sb("a3", [K3, GROUPS, STRIPS, W], BF16)
        h = sb("h", [P, RING * STRIPS, W])
        x2 = sb("x2", [P, GROUPS, W])
        x2T = sb("x2T", [P, GROUPS, W])
        r1 = sb("r1", [P, GROUPS, W])
        y = sb("y", [P, GROUPS, W])

        z_ps = [bank(f"z_ps{s}") for s in range(STRIPS)]
        sum_ps = bank("sum_ps")
        turn_ps = bank("turn_ps")
        lin_ps = bank("lin_ps")
        end_ps = bank("end_ps")

        def per_group(name):
            return [sem(f"{name}{g}") for g in range(GROUPS)]

        s_x = per_group("s_x_in")
        s_q = [sem(f"s_q{layer}") for layer in range(2)]
        s_id = sem("s_id")
        s_wl = [sem(f"s_wl{n}") for n in range(3)]
        s_b = sem("s_b")
        s_pick = sem("s_pick")
        s_a3 = [[sem(f"s_a3_{g}{s}") for s in range(STRIPS)] for g in range(GROUPS)]
        s_out = sem("s_out")
        s_warm = sem("s_warm")
        s_aT = sem("s_aT")
        s_add = sem("s_add")
        s_relu = sem("s_relu")
        s_add_up = sem("s_add_up")
        s_qe_ps = sem("s_qe_ps")
        s_lin0 = sem("s_lin0")
        s_lin1 = sem("s_lin1")
        s_z = sem("s_z")
        s_sum = sem("s_sum")
        s_turn2 = sem("s_turn2")
        s_lin2 = sem("s_lin2")
        s_lin2_own = sem("s_lin2_own")
        s_q_lin = sem("s_q_lin")
        s_qe = sem("s_qe")
        s_x_sum = sem("s_x_sum")
        s_x_mix = sem("s_x_mix")
        s_zT = per_group("s_zT")
        s_half = sem("s_half")
        s_r0 = sem("s_r0")
        s_x1 = per_group("s_x1")
        s_uT = per_group("s_uT")
        s_a = sem("s_a")
        s_hi = per_group("s_hi")
        s_diag = per_group("s_diag")
        s_rest = per_group("s_rest")
        s_mid = per_group("s_mid")
        s_lo = per_group("s_lo")
        s_h_act = sem("s_h_act")
        s_h_dve = sem("s_h_dve")
        s_x2 = sem("s_x2")
        s_x2T = per_group("s_x2T")
        s_r1 = sem("s_r1")
        s_y = per_group("s_y")
        s_r1_own = sem("s_r1_own")

        def gate(layer, g):
            v = qe[:, layer, :, GB * g:GB * (g + 1)]
            return v.unsqueeze(3).to_broadcast([P, KD, GB, N])

        def by_batch(ap):
            return ap.rearrange("p (k b i) -> p k b i", k=KD, b=GB)

        def tile_of(buf, g, t):
            return buf[:, g, t * D:(t + 1) * D]

        def rows_of(buf, g, t):
            return buf[:, g, :].rearrange("p (k r) -> p k r", k=KD)[:, :, t * P:(t + 1) * P]

        def by_half(ap):
            return ap.rearrange("p (k r) -> p k r", k=KD)

        def b2(layer, k):
            at = BATCHES + 2 * KD + layer * KD + k
            return q_sb[:, at:at + 1]

        def lin0_ps(g):
            return end_ps if g % 2 == 0 else turn_ps

        def lin1_ps(g):
            return lin_ps if g % 2 == 0 else (sum_ps if g == 1 else end_ps)

        turn_end = [z_ps[0], z_ps[1]]
        lin_end = [z_ps[2], z_ps[3]]
        own_ps = [lin_ps, turn_ps]

        block = ctx.enter_context(nc.Block())

        @block.sync
        def _(sp):
            def weight(n):
                sp.dma_start(wl_sb[:, n, :, :], w_lin[n].rearrange("(k p) e -> p k e", p=P)).then_inc(s_wl[n], 16)

            sp.dma_start(q_sb[:, 0:Q0], q_pack[:, 0:Q0]).then_inc(s_q[0], 16)
            weight(0)
            sp.dma_start(q_sb[:, Q0:], q_pack[:, Q0:]).then_inc(s_q[1], 16)
            weight(1)
            sp.dma_start(b1_sb[:, :], b1.partition_broadcast(P)).then_inc(s_b, 16)
            sp.dma_start(pick_sb[:, :, :], pick_m).then_inc(s_pick, 16)
            sp.dma_start(gather_sb[:, :, :], gather_m).then_inc(s_pick, 16)
            sp.dma_start(id_sb[:, :], ident_m).then_inc(s_id, 16)
            weight(2)
            for g in PAIRED:
                sp.wait_ge(s_lo[g], 1)
                for s in range(STRIPS):
                    sp.dma_start(a3[:, g, s, :],
                                 a_parts[s * N:(s + 1) * N, g, :, :]).then_inc(s_a3[g][s], 16)
            for g in PAIRED[:-1]:
                sp.wait_ge(s_y[g], 1)
                sp.dma_start(outT[:, g, :], y[:, g, :]).then_inc(s_out, 16)
            sp.wait_ge(s_y[OWN], 1)
            sp.dma_start(outT[:, OWN, :], y[:, OWN, :]).then_inc(s_out, 16)
            for t in range(PER):
                sp.wait_ge(s_y[LAST], t + 1)
                sp.dma_start(outT[:, LAST, :].rearrange("p (k r) -> p k r", k=KD)[:, :, t * P:(t + 1) * P],
                             rows_of(y, LAST, t)).then_inc(s_out, 16)
            sp.wait_ge(s_out, 16 * (LAST + PER))

        @block.gpsimd
        def _(pool):
            nc.gpsimd.memset(warm_sb[:, :], 1.0).then_inc(s_warm, 1)
            for name, g in POOL:
                if name == "z":
                    pool.wait_ge(s_x_mix, g + 1)
                    pool.wait_ge(s_qe, 1)
                    nc.gpsimd.tensor_tensor(by_batch(zT[:, g, :]), by_batch(x_mix[:, g, :]), gate(0, g),
                                            ALU.mult).then_inc(s_zT[g], 1)
                if name == "x1":
                    pool.wait_ge(s_r0, g + 1)
                    nc.gpsimd.tensor_tensor(x1[:, g, :], r0[:, g, :], x_sb[:, g, :], ALU.add).then_inc(s_x1[g], 1)
                if name == "u":
                    pool.wait_ge(s_x1[g], 1)
                    pool.wait_ge(s_qe, 2)
                    nc.gpsimd.tensor_tensor(by_batch(uT[:, g, :]), by_batch(x1[:, g, :]), gate(1, g),
                                            ALU.mult).then_inc(s_uT[g], 1)
                if name == "rest":
                    pool.wait_ge(s_hi[g], 1)
                    nc.gpsimd.tensor_tensor(a_rest[:, g, :], a[:, g, :], a_hi[:, g, :],
                                            ALU.subtract).then_inc(s_rest[g], 1)
                if name == "lo":
                    pool.wait_ge(s_rest[g], 1)
                    pool.wait_ge(s_mid[g], 1)
                    nc.gpsimd.tensor_tensor(a_lo[:, g, :], a_rest[:, g, :], a_mid[:, g, :],
                                            ALU.subtract).then_inc(s_lo[g], 1)
                if name == "y":
                    pool.wait_ge(s_r1, nth(g))
                    nc.gpsimd.tensor_tensor(y[:, g, :], r1[:, g, :], x1[:, g, :], ALU.add).then_inc(s_y[g], 1)
                if name == "y_own":
                    pool.wait_ge(s_r1_own, KD)
                    nc.gpsimd.tensor_tensor(y[:, OWN, :], r1[:, OWN, :], x1[:, OWN, :], ALU.add).then_inc(s_y[OWN], 1)
                if name == "pair":
                    rows = aT[:, g * N:(g + 1) * N]
                    if g == 0:
                        pool.wait_ge(s_aT, 1)
                    if g == GB:
                        pool.wait_ge(s_aT, KD)
                    if g >= SLOTS:
                        pool.wait_ge(s_add_up, g - SLOTS + 1)
                    nc.gpsimd.tensor_tensor(pairs[:, g % SLOTS, :, :],
                                            rows.unsqueeze(2).to_broadcast([P, N, N]),
                                            rows.unsqueeze(1).to_broadcast([P, N, N]),
                                            ALU.add).then_inc(s_add, 1)

        @block.scalar
        def _(act):
            for g in range(GROUPS):
                act.dma_start(x_sb[:, g, :], xT[:, g, :]).then_inc(s_x[g], 16)

            def step(name, g):
                if name == "lin0":
                    act.wait_ge(s_lin0, g + 1)
                    for k in range(KD):
                        last = nc.scalar.activation(r0[:, g, k * GR:(k + 1) * GR],
                                                    lin0_ps(g)[:, k * GR:(k + 1) * GR], ACT.Relu, bias=b2(0, k))
                    last.then_inc(s_r0, 1)
                if name == "hi":
                    act.wait_ge(s_a, nth(g))
                    nc.scalar.copy(a_hi[:, g, :], a[:, g, :]).then_inc(s_hi[g], 1)
                if name == "mid":
                    act.wait_ge(s_rest[g], 1)
                    nc.scalar.copy(a_mid[:, g, :], a_rest[:, g, :]).then_inc(s_mid[g], 1)
                if name == "diag":
                    act.wait_ge(s_a, nth(g))
                    nc.scalar.activation(diag[:, g, :], a[:, g, :], ACT.Relu, scale=2.0).then_inc(s_diag[g], 1)
                if name == "relu":
                    act.wait_ge(s_add, g + 1)
                    nc.scalar.activation(pairs[:, g % SLOTS, :, :], pairs[:, g % SLOTS, :, :],
                                         ACT.Relu).then_inc(s_relu, 1)
                if name == "aT":
                    act.wait_ge(s_half, 2)
                    act.wait_ge(s_lin1, OWN + 1)
                    for k in range(KD):
                        nc.scalar.activation(aT[:, k * GR:(k + 1) * GR], lin1_ps(OWN)[:, k * GR:(k + 1) * GR],
                                             ACT.Identity, bias=half_b1c[:, k:k + 1]).then_inc(s_aT, 1)
                if name == "turn2":
                    act.wait_ge(s_turn2, nth(g))
                    nc.scalar.copy(x2T[:, g, :], turn_ps[:, :]).then_inc(s_x2T[g], 1)
                if name == "lin2":
                    act.wait_ge(s_lin2, nth(g))
                    for k in range(KD):
                        last = nc.scalar.activation(r1[:, g, k * GR:(k + 1) * GR], end_ps[:, k * GR:(k + 1) * GR],
                                                    ACT.Relu, bias=b2(1, k))
                    last.then_inc(s_r1, 1)
                if name == "own":
                    act.wait_ge(s_lin2_own, g + 1)
                    nc.scalar.activation(r1[:, OWN, g * GR:(g + 1) * GR], own_ps[g][:, 0:GR], ACT.Relu,
                                         bias=b2(1, g)).then_inc(s_r1_own, 1)
                if name == "turn_end":
                    act.wait_ge(s_turn2, nth(LAST) + g)
                    nc.scalar.copy(rows_of(x2T, LAST, g), by_half(turn_end[g][:, 0:D])).then_inc(s_x2T[LAST], 1)
                if name == "lin_end":
                    act.wait_ge(s_lin2, nth(LAST) + g)
                    for k in range(KD):
                        last = nc.scalar.activation(rows_of(r1, LAST, g)[:, k, :],
                                                    lin_end[g][:, k * P:(k + 1) * P], ACT.Relu, bias=b2(1, k))
                    last.then_inc(s_r1, 1)

            def quad(k):
                for s in range(STRIPS):
                    if on_scalar(k, s):
                        act.wait_ge(s_z, STRIPS * k + s + 1)
                        if k >= RING:
                            act.wait_ge(s_sum, k - RING + 1)
                        nc.scalar.activation(h[:, k % RING * STRIPS + s, :], z_ps[s][:, :],
                                             ACT.Relu).then_inc(s_h_act, 1)

            for st in SCALAR_LEAD:
                step(*st)
            quad(0)
            for k in range(-1, QUADS):
                if 0 <= k < QUADS - 1:
                    quad(k + 1)
                for st in SCALAR.get(k, []):
                    step(*st)
            for st in SCALAR_TAIL:
                step(*st)

        @block.vector
        def _(dve):
            def gates(layer, bank):
                b3 = q_sb[:, BATCHES + layer * KD:BATCHES + (layer + 1) * KD]
                dve.wait_ge(s_qe_ps, layer + 1)
                nc.vector.tensor_tensor(q_lin[:, layer, :, :],
                                        by_half(bank[:, 0:KD * P])[:, :, 0:BATCHES],
                                        b3.unsqueeze(2).to_broadcast([P, KD, BATCHES]),
                                        ALU.add).then_inc(s_q_lin, 1)
                dve.wait_ge(s_q_lin, layer + 1)
                nc.vector.tensor_scalar(qe[:, layer, :, :], q_lin[:, layer, :, :], 0.0, None,
                                        ALU.max).then_inc(s_qe, 1)

            def step(name, g):
                if name == "sum":
                    dve.wait_ge(s_x[g], 16)
                    nc.vector.tensor_reduce(x_sum[:, g, :], x_sb[:, g, :].rearrange("p (m i) -> p m i", i=N),
                                            mybir.AxisListType.X, ALU.add).then_inc(s_x_sum, 1)
                if name == "mix":
                    dve.wait_ge(s_x_sum, g + 1)
                    nc.vector.scalar_tensor_tensor(
                        out=x_mix[:, g, :].rearrange("p (m i) -> p m i", i=N),
                        in0=x_sb[:, g, :].rearrange("p (m i) -> p m i", i=N), scalar=float(N),
                        in1=x_sum[:, g, :].unsqueeze(2).to_broadcast([P, KD * GB, N]), op0=ALU.mult,
                        op1=ALU.add).then_inc(s_x_mix, 1)
                if name == "gate":
                    gates(g, (sum_ps, lin_ps)[g])
                if name == "half":
                    dve.wait_ge(s_b, 16)
                    nc.vector.tensor_scalar(half_b1[:, :], b1_sb[:, :], 0.5, None, ALU.mult).then_inc(s_half, 1)
                    at = BATCHES + 4 * KD
                    nc.vector.tensor_scalar(half_b1c[:, :], q_sb[:, at:at + KD], 0.5, None,
                                            ALU.mult).then_inc(s_half, 1)
                if name == "a":
                    dve.wait_ge(s_half, 2)
                    dve.wait_ge(s_lin1, g + 1)
                    nc.vector.tensor_tensor(a[:, g, :].rearrange("p (t d) -> p t d", t=PER),
                                            lin1_ps(g)[:, :].rearrange("p (t d) -> p t d", t=PER),
                                            half_b1[:, :].unsqueeze(1).to_broadcast([P, PER, D]),
                                            ALU.add).then_inc(s_a, 1)
                if name == "aT":
                    dve.wait_ge(s_half, 2)
                    dve.wait_ge(s_lin1, OWN + 1)
                    nc.vector.tensor_tensor(by_half(aT[:, :]), by_half(lin1_ps(OWN)[:, :]),
                                            half_b1c[:, :].unsqueeze(2).to_broadcast([P, KD, GR]),
                                            ALU.add).then_inc(s_aT, KD)
                if name == "add_up":
                    dve.wait_ge(s_relu, g + 1)
                    nc.vector.tensor_reduce(x2T[:, OWN, g * N:(g + 1) * N], pairs[:, g % SLOTS, :, :],
                                            mybir.AxisListType.X, ALU.add).then_inc(s_add_up, 1)
                if name == "x2":
                    dve.wait_ge(s_sum, CHUNKS * nth(g))
                    dve.wait_ge(s_diag[g], 1)
                    if g < LAST:
                        nc.vector.tensor_tensor(x2[:, g, :], sum_ps[:, :], diag[:, g, :],
                                                ALU.add).then_inc(s_x2, 1)
                    else:
                        for t in range(PER):
                            nc.vector.tensor_tensor(tile_of(x2, g, t), sum_ps[:, t * D:(t + 1) * D],
                                                    tile_of(diag, g, t), ALU.add).then_inc(s_x2, 1)
                if name == "z":
                    dve.wait_ge(s_x_mix, g + 1)
                    dve.wait_ge(s_qe, 1)
                    nc.vector.tensor_tensor(by_batch(zT[:, g, :]), by_batch(x_mix[:, g, :]), gate(0, g),
                                            ALU.mult).then_inc(s_zT[g], 1)
                if name == "x1":
                    dve.wait_ge(s_r0, g + 1)
                    nc.vector.tensor_tensor(x1[:, g, :], r0[:, g, :], x_sb[:, g, :], ALU.add).then_inc(s_x1[g], 1)
                if name == "u":
                    dve.wait_ge(s_x1[g], 1)
                    dve.wait_ge(s_qe, 2)
                    nc.vector.tensor_tensor(by_batch(uT[:, g, :]), by_batch(x1[:, g, :]), gate(1, g),
                                            ALU.mult).then_inc(s_uT[g], 1)
                if name == "rest":
                    dve.wait_ge(s_hi[g], 1)
                    nc.vector.tensor_tensor(a_rest[:, g, :], a[:, g, :], a_hi[:, g, :],
                                            ALU.subtract).then_inc(s_rest[g], 1)
                if name == "lo":
                    dve.wait_ge(s_rest[g], 1)
                    dve.wait_ge(s_mid[g], 1)
                    nc.vector.tensor_tensor(a_lo[:, g, :], a_rest[:, g, :], a_mid[:, g, :],
                                            ALU.subtract).then_inc(s_lo[g], 1)
                if name == "y":
                    dve.wait_ge(s_r1, nth(g))
                    nc.vector.tensor_tensor(y[:, g, :], r1[:, g, :], x1[:, g, :], ALU.add).then_inc(s_y[g], 1)
                if name == "y_own":
                    dve.wait_ge(s_r1_own, KD)
                    nc.vector.tensor_tensor(y[:, OWN, :], r1[:, OWN, :], x1[:, OWN, :], ALU.add).then_inc(s_y[OWN], 1)
                if name == "hi":
                    dve.wait_ge(s_a, nth(g))
                    nc.vector.tensor_copy(a_hi[:, g, :], a[:, g, :]).then_inc(s_hi[g], 1)
                if name == "mid":
                    dve.wait_ge(s_rest[g], 1)
                    nc.vector.tensor_copy(a_mid[:, g, :], a_rest[:, g, :]).then_inc(s_mid[g], 1)
                if name == "diag":
                    dve.wait_ge(s_a, nth(g))
                    nc.vector.tensor_scalar(diag[:, g, :], a[:, g, :], 2.0, 0.0, ALU.mult,
                                            ALU.max).then_inc(s_diag[g], 1)
                if name == "y_end":
                    dve.wait_ge(s_r1, nth(LAST) + g)
                    nc.vector.tensor_tensor(rows_of(y, LAST, g), rows_of(r1, LAST, g), rows_of(x1, LAST, g),
                                            ALU.add).then_inc(s_y[LAST], 1)

            def quad(k):
                for s in range(STRIPS):
                    if not on_scalar(k, s):
                        dve.wait_ge(s_z, STRIPS * k + s + 1)
                        if k >= RING:
                            dve.wait_ge(s_sum, k - RING + 1)
                        nc.vector.tensor_scalar(h[:, k % RING * STRIPS + s, :], z_ps[s][:, :], 0.0, None,
                                                ALU.max).then_inc(s_h_dve, 1)

            for st in VECTOR_LEAD:
                step(*st)
            quad(0)
            for k in range(-1, QUADS):
                if 0 <= k < QUADS - 1:
                    quad(k + 1)
                for st in VECTOR.get(k, []):
                    step(*st)
            for st in VECTOR_TAIL:
                step(*st)

        @block.tensor
        def _(pe):
            def to_features(out, rhs, n, half, parts=range(KD)):
                for k in parts:
                    mm = nc.tensor.matmul(out, wl_sb[:, n, k, half * P:(half + 1) * P], rhs[:, k, :],
                                          start=(k == 0), stop=(k == KD - 1))
                return mm

            def to_rows(out, lhs, n, g, t):
                for k in range(KD):
                    mm = nc.tensor.matmul(out, lhs[:, g, (k * PER + t) * P:(k * PER + t + 1) * P],
                                          wl_sb[:, n, k, :], start=(k == 0), stop=(k == KD - 1))
                return mm

            def features(bank, src, n, g):
                for half in range(KD):
                    mm = to_features(bank[:, half * GR:(half + 1) * GR], by_half(src[:, g, :]), n, half)
                return mm

            def turn(bank, src, g, t, k, col):
                return nc.tensor.transpose(bank[:, col * P:(col + 1) * P],
                                           src[:, g, t * D + k * P:t * D + (k + 1) * P], id_sb[:, :])

            def turns(bank, src, g):
                for k in range(KD):
                    for t in range(PER):
                        mm = turn(bank, src, g, t, k, k * PER + t)
                return mm

            def gates(bank, w):
                q_wide = q_sb[:, 0:BATCHES].unsqueeze(1).to_broadcast([Q, P // BATCHES, BATCHES])
                for k in range(KD):
                    mm = nc.tensor.matmul(bank[:, k * P:(k + 1) * P], w[:, k * P:(k + 1) * P], q_wide,
                                          start=True, stop=True)
                mm.then_inc(s_qe_ps, 1)

            def step(name, g):
                if name == "warm":
                    for _ in range(g):
                        nc.tensor.matmul(end_ps[:, :], warm_sb[:, 0:P], warm_sb[:, :], start=True, stop=True)
                if name == "gate":
                    pe.wait_ge(s_q[g], 16)
                    gates((sum_ps, lin_ps)[g], q_sb[:, Q0 - D:Q0] if g == 0 else q_sb[:, Q0:])
                if name == "lin0":
                    if g == 0:
                        pe.wait_ge(s_wl[0], 16)
                    if g >= 2:
                        pe.wait_ge(s_r0, g - 1)
                    pe.wait_ge(s_zT[g], 1)
                    features(lin0_ps(g), zT, 0, g).then_inc(s_lin0, 1)
                if name == "lin1":
                    if g == 0:
                        pe.wait_ge(s_wl[1], 16)
                        pe.wait_ge(s_q_lin, 2)
                    if g == 2:
                        pe.wait_ge(s_aT, KD)
                    if g == 3:
                        pe.wait_ge(s_r0, 3)
                    pe.wait_ge(s_uT[g], 1)
                    if g == OWN:
                        mm = features(lin1_ps(g), uT, 1, g)
                    else:
                        for t in range(PER):
                            mm = to_rows(lin1_ps(g)[:, t * D:(t + 1) * D], uT, 1, g, t)
                    mm.then_inc(s_lin1, 1)
                if name == "turn2":
                    if nth(g) == 1:
                        pe.wait_ge(s_id, 16)
                        pe.wait_ge(s_r0, GROUPS)
                    else:
                        pe.wait_ge(s_x2T[PAIRED[nth(g) - 2]], 1)
                    pe.wait_ge(s_x2, nth(g))
                    turns(turn_ps, x2, g).then_inc(s_turn2, 1)
                if name == "lin2":
                    if nth(g) == 1:
                        pe.wait_ge(s_wl[2], 16)
                        pe.wait_ge(s_a, nth(LAST))
                    else:
                        pe.wait_ge(s_r1, nth(g) - 1)
                    pe.wait_ge(s_x2T[g], 1)
                    features(end_ps, x2T, 2, g).then_inc(s_lin2, 1)
                if name == "own":
                    k, half = g // KD, g % KD
                    if g == 0:
                        pe.wait_ge(s_wl[2], 16)
                        pe.wait_ge(s_a, 2)
                    if g == 1:
                        pe.wait_ge(s_x2T[PAIRED[-2]], 1)
                    pe.wait_ge(s_add_up, (k + 1) * GB)
                    mm = to_features(own_ps[half][:, 0:GR], by_half(x2T[:, OWN, :]), 2, half, [k])
                    if k == KD - 1:
                        mm.then_inc(s_lin2_own, 1)
                if name == "turn_end":
                    if g == 0:
                        pe.wait_ge(s_h_act, relus(QUADS - 1, STRIPS - 1, True))
                        pe.wait_ge(s_h_dve, relus(QUADS - 1, STRIPS - 1, False))
                    pe.wait_ge(s_x2, nth(LAST) + g)
                    for k in range(KD):
                        mm = turn(turn_end[g], x2, LAST, g, k, k)
                    mm.then_inc(s_turn2, 1)
                if name == "lin_end":
                    pe.wait_ge(s_x2T[LAST], g + 1)
                    for half in range(KD):
                        mm = to_features(lin_end[g][:, half * P:(half + 1) * P], rows_of(x2T, LAST, g), 2, half)
                    mm.then_inc(s_lin2, 1)

            def pair_sums(k):
                g, c = PAIRED[k // CHUNKS], k % CHUNKS
                if k == 0:
                    pe.wait_ge(s_pick, 32)
                for s in range(STRIPS):
                    if c == 0:
                        pe.wait_ge(s_a3[g][s], 16)
                    if k >= 1:
                        who = on_scalar(k - 1, s)
                        pe.wait_ge(s_h_act if who else s_h_dve, relus(k - 1, s, who))
                    nc.tensor.matmul(z_ps[s][:, :], pick_sb[:, c, :], a3[:, g, s, :], start=True,
                                     stop=True).then_inc(s_z, 1)

            def sum_pairs(k):
                g, c = PAIRED[k // CHUNKS], k % CHUNKS
                if k == 0:
                    pe.wait_ge(s_a, 1)
                if c == 0 and k > 0:
                    pe.wait_ge(s_x2, nth(g) - 1)
                for s in range(STRIPS):
                    who = on_scalar(k, s)
                    pe.wait_ge(s_h_act if who else s_h_dve, relus(k, s, who))
                    mm = nc.tensor.matmul(sum_ps[s * N:(s + 1) * N, :], gather_sb[:, c, :],
                                          h[:, k % RING * STRIPS + s, :], start=(c == 0),
                                          stop=(c == CHUNKS - 1))
                mm.then_inc(s_sum, 1)

            pe.wait_ge(s_warm, 1)
            for st in TENSOR_LEAD:
                step(*st)
            pair_sums(0)
            for k in range(-1, QUADS):
                if 0 <= k < QUADS - 1:
                    pair_sums(k + 1)
                for st in TENSOR.get(k, []):
                    step(*st)
                if k >= 0:
                    sum_pairs(k)
            for st in TENSOR_TAIL:
                step(*st)


def constants():
    import numpy as np

    pairs = [(i, j) for i in range(N) for j in range(i + 1, N)]
    pick = np.zeros((K3, CHUNKS, P), mybir.dt.np(BF16))
    gather = np.zeros((P, CHUNKS, N), np.float32)
    for n, pair in enumerate(pairs):
        c, p = n // PC, n % PC
        for row in pair:
            pick[row * PARTS:(row + 1) * PARTS, c, p] = 1
            gather[p, c, row] = 1
    return np.eye(P, dtype=np.float32), pick, gather


def kernel(x, cond_1024, L0_cond_W3, L0_cond_b3, L0_cond_W2, L0_cond_b2, L1_cond_W1, L1_cond_b1,
           L1_cond_W2, L1_cond_b2, L1_cond_W3, L1_cond_b3):
    import numpy as np
    import concourse.bacc as bacc
    from concourse.bass_utils import run_bass_kernel_spmd

    ident, pick, gather = constants()
    columns = np.concatenate([L0_cond_b3, L1_cond_b3, L0_cond_b2, L1_cond_b2, L1_cond_b1]).reshape(5 * KD, P).T
    x_groups = np.asarray(x).reshape(GROUPS, GR, KD, P)
    arrays = {
        "xT_in": np.ascontiguousarray(x_groups.transpose(3, 0, 2, 1)).reshape(P, GROUPS, W),
        "q_pack_in": np.concatenate([np.asarray(cond_1024).T, columns, np.asarray(L0_cond_W3),
                                     np.asarray(L1_cond_W3)], axis=1),
        "b1_in": np.ascontiguousarray(L1_cond_b1),
        "w_lin_in": np.stack([L0_cond_W2, L1_cond_W1, L1_cond_W2]),
        "ident_in": ident,
        "pick_in": pick,
        "gather_in": gather,
    }
    nc = bacc.Bacc("TRN2", target_bir_lowering=False, num_devices=1)
    args = [nc.dram_tensor(name, a.shape, mybir.dt.from_np(a.dtype), kind="ExternalInput").ap()
            for name, a in arrays.items()]
    args.append(nc.dram_tensor("outT", (P, GROUPS, W), F32, kind="ExternalOutput").ap())
    build(nc, *args)
    r = run_bass_kernel_spmd(nc, [arrays], core_ids=[0])
    groups = r.results[0]["outT"].reshape(P, GROUPS, KD, GR)
    return np.ascontiguousarray(groups.transpose(1, 3, 2, 0)).reshape(BATCHES, N, D)
```
